# Optimizing a Trainium2 kernel written in Bass

```python
import numpy as np
import jax
import jax.numpy as jnp

def _softmax(x, axis=-1):
    return jax.nn.softmax(x, axis=axis)

def _gelu(x):
    return jax.nn.gelu(x, approximate=True)

def _silu(x):
    return jax.nn.silu(x)

def _sigmoid(x):
    return jax.nn.sigmoid(x)

def _layernorm(x, axis=-1, eps=1e-05):
    m = jnp.mean(x, axis=axis, keepdims=True)
    v = jnp.var(x, axis=axis, keepdims=True)
    return (x - m) / jnp.sqrt(v + eps)

def _scatter_add(tgt, idx, src, axis=0):
    return tgt.at[idx].add(src)

def _segment_sum(src, seg, n):
    return jax.ops.segment_sum(src, seg, n)
kernel_name = 'mk_adj_preln_d1_adj_r2_c2107b'

def setup_inputs(seed: int=0):
    np.random.seed(seed)
    _w = jnp.asarray

    def _rec_inputs():
        import jax
        import jax.numpy as jnp
        _gk = jax.random.key(seed)
        x = -0.0001538 + 1 * jax.random.normal(jax.random.fold_in(_gk, 1), (128, 128, 384), jnp.float32)
        _a = jax.random.bernoulli(jax.random.fold_in(_gk, 2), 0.03125, (128, 128, 128))
        _a = jnp.logical_or(_a, jnp.eye(128, dtype=bool))
        adj = _a
        return (x, adj)
    x, adj = _rec_inputs()

    def _L0_gnn_setup():
        import jax, jax.numpy as jnp
        import numpy as np
        B, S, H = (4, 1024, 384)
        NUM_HEADS = 6
        HEAD_SIZE = H // NUM_HEADS
        NEG = -9000000000000000.0

        def _heads(x):
            b, s, _ = x.shape
            return x.reshape(b, s, NUM_HEADS, HEAD_SIZE).transpose(0, 2, 1, 3)
        key = jax.random.key(seed)
        ks = jax.random.split(key, 10)
        seq_inputs = jax.random.normal(ks[0], (B, S, H), dtype=jnp.float32)
        gm = jax.random.randint(ks[1], (B, S, S), 0, 2) > 0
        graph_mask = gm | jnp.eye(S, dtype=bool)[None]
        sc = 1.0 / np.sqrt(H)
        Wq = jax.random.normal(ks[2], (H, H), dtype=jnp.float32) * sc
        bq = jnp.zeros((H,), dtype=jnp.float32)
        Wk = jax.random.normal(ks[3], (H, H), dtype=jnp.float32) * sc
        bk = jnp.zeros((H,), dtype=jnp.float32)
        Wv = jax.random.normal(ks[4], (H, H), dtype=jnp.float32) * sc
        bv = jnp.zeros((H,), dtype=jnp.float32)
        Wf = jax.random.normal(ks[5], (H, H), dtype=jnp.float32) * sc
        bf = jnp.zeros((H,), dtype=jnp.float32)
        return {'seq_inputs': seq_inputs, 'Wq': Wq, 'bq': bq, 'Wk': Wk, 'bk': bk, 'Wv': Wv, 'bv': bv, 'Wf': Wf, 'bf': bf, 'graph_mask': graph_mask}
    _L0_gnn_all = _L0_gnn_setup()
    _L0_gnn_in = {k: v for k, v in _L0_gnn_all.items() if k in ('Wq', 'bq', 'Wk', 'bk', 'Wv', 'bv', 'Wf', 'bf')}
    del _L0_gnn_all
    return {'x': x, 'adj': adj, 'L0_gnn_Wq': _L0_gnn_in['Wq'], 'L0_gnn_bq': _L0_gnn_in['bq'], 'L0_gnn_Wk': _L0_gnn_in['Wk'], 'L0_gnn_bk': _L0_gnn_in['bk'], 'L0_gnn_Wv': _L0_gnn_in['Wv'], 'L0_gnn_bv': _L0_gnn_in['bv'], 'L0_gnn_Wf': _L0_gnn_in['Wf'], 'L0_gnn_bf': _L0_gnn_in['bf']}

def reference(x, adj, L0_gnn_Wq, L0_gnn_bq, L0_gnn_Wk, L0_gnn_bk, L0_gnn_Wv, L0_gnn_bv, L0_gnn_Wf, L0_gnn_bf):
    import jax
    import jax.numpy as jnp

    def _L0_gnn_ref(seq_inputs, Wq, bq, Wk, bk, Wv, bv, Wf, bf, graph_mask):
        import jax, jax.numpy as jnp
        import numpy as np
        B, S, H = (4, 1024, 384)
        NUM_HEADS = 6
        HEAD_SIZE = H // NUM_HEADS
        NEG = -9000000000000000.0

        def _heads(x):
            b, s, _ = x.shape
            return x.reshape(b, s, NUM_HEADS, HEAD_SIZE).transpose(0, 2, 1, 3)
        q = _heads(seq_inputs @ Wq + bq)
        k = _heads(seq_inputs @ Wk + bk)
        v = _heads(seq_inputs @ Wv + bv)
        scores = jnp.einsum('bhqd,bhkd->bhqk', q, k) / np.sqrt(HEAD_SIZE)
        bias = jnp.where(graph_mask, 0.0, NEG)[:, None]
        probs = jax.nn.softmax(scores + bias, axis=-1)
        ctx = jnp.einsum('bhqk,bhkd->bhqd', probs, v)
        ctx = ctx.transpose(0, 2, 1, 3).reshape(seq_inputs.shape[0], seq_inputs.shape[1], H)
        return ctx @ Wf + bf
    h = jnp.maximum(_layernorm(x, axis=-1), 0.0)
    x = x + _L0_gnn_ref(h, L0_gnn_Wq, L0_gnn_bq, L0_gnn_Wk, L0_gnn_bk, L0_gnn_Wv, L0_gnn_bv, L0_gnn_Wf, L0_gnn_bf, adj)
    return x

_drawn_inputs = setup_inputs


def setup_inputs(seed=0):
    import zlib

    import numpy as np

    out = dict(_drawn_inputs(seed))
    spreads = {'L0_gnn_bq': (0.0, 0.67),
     'L0_gnn_bk': (0.0, 0.8),
     'L0_gnn_bv': (0.0, 0.1),
     'L0_gnn_bf': (0.0, 0.1)}
    factors = {}
    for name, (base, spread) in spreads.items():
        noise = np.random.default_rng([zlib.crc32(name.encode()), seed]).standard_normal(out[name].shape)
        drawn = base * np.exp(spread * noise) if base else spread * noise
        out[name] = jnp.asarray(drawn.astype(out[name].dtype))
    for name, factor in factors.items():
        out[name] = (out[name] * factor).astype(out[name].dtype)
    return out
```

```python
from contextlib import ExitStack

import concourse.bass as bass
from concourse import mybir

F32 = mybir.dt.float32
F32R = mybir.dt.float32r
U8 = mybir.dt.uint8
ALU = mybir.AluOpType
ACT = mybir.ActivationFunctionType

P = 128
RING = 8
GROUP = 4
LEAD_H = 8
LEAD_V = 4
LEAD_X = 3
NORM_EPS = 1e-5
MASKED = 9000000000000000.0


def bass_preln_graph_attention(nc, x, adj, Wq, bq, Wk, bk, Wv, bv, Wf, bf, out):
    B, S, H = x.shape
    C = H // P
    D = 64
    NH = H // D
    HALF = NH // 2
    ROOT = 0.125
    O_RING = 4
    TILES = 2 * C
    SHARE = [[0], [1, 2], [3, 4], [5]]
    assert S == P and H == C * P and C == 3 and D * NH == H and B % RING == 0

    START, FIRST = -LEAD_H, GROUP
    LOOPS = (B - LEAD_H - FIRST) // RING
    AFTER, END = FIRST + RING * LOOPS, B + 1

    with ExitStack() as ctx:
        def sb(name, shape, dt=F32):
            return ctx.enter_context(nc.sbuf_tensor(name, shape, dt))

        def psum(name, shape):
            return ctx.enter_context(nc.psum_tensor(name, shape, F32))

        def sem(name):
            return ctx.enter_context(nc.semaphore(name))

        w_raw = sb("w_raw", [P, 4, C, H])
        w_hi = sb("w_hi", [P, 4, C, H], F32R)
        w_lo = sb("w_lo", [P, 4, C, H], F32R)
        bias_qk = sb("bias_qk", [P, TILES])
        bv_rows = sb("bv_rows", [P, H])
        bf_rows = sb("bf_rows", [P, H])
        ident = sb("ident", [P, P])
        minus_half = sb("minus_half", [P, 1])
        x_in = sb("x_in", [P, RING, H])
        x_bf = sb("x_bf", [P, RING, H])
        h_rows = sb("h_rows", [P, 2, H])
        hT_hi = sb("hT_hi", [P, C, RING, P], F32R)
        hT_lo = sb("hT_lo", [P, C, RING, P], F32R)
        qkT = sb("qkT", [P, TILES, 2, GROUP * P])
        v_rows = sb("v_rows", [P, RING, H])
        adj_in = sb("adj_in", [P, 2, GROUP, P], U8)
        mask = sb("mask", [P, 2, P])
        neg_scores = sb("neg_scores", [P, NH, P])
        neg_max = sb("neg_max", [P, NH])
        probs = sb("probs", [P, NH, P])
        row_sum = sb("row_sum", [P, NH])
        inv_sum = sb("inv_sum", [P, NH])
        probs_n = sb("probs_n", [P, NH, P])
        pT = sb("pT", [P, 2, NH, P])
        cT_hi = sb("cT_hi", [P, 2, C, P], F32R)
        cT_lo = sb("cT_lo", [P, 2, C, P], F32R)
        out_rows = sb("out_rows", [P, O_RING, H])
        bn = sb("bn", [P, 2, 6])
        mean_var = sb("mean_var", [P, 2, 2])
        var_eps = sb("var_eps", [P, 2, 1])
        rstd = sb("rstd", [P, 2, 1])
        shift = sb("shift", [P, 2, 1])

        ps_even = psum("ps_even", [P, 512])
        ps_odd = psum("ps_odd", [P, 512])
        ps_pT = psum("ps_pT", [P, 2, 512])
        ps_ctx = psum("ps_ctx", [P, 512])
        ps_hT = psum("ps_hT", [P, 512])
        ps_v = psum("ps_v", [P, 512])
        ps_qk = psum("ps_qk", [P, 512])

        w_loaded = [sem(f"w_loaded{i}") for i in range(4)]
        b_loaded = sem("b_loaded")
        x_loaded = [sem(f"x_loaded{i}") for i in range(RING)]
        adj_loaded = [sem(f"adj_loaded{i}") for i in range(2)]
        out_stored = [sem(f"out_stored{i}") for i in range(O_RING)]
        zeroed = sem("zeroed")
        consts_ready = sem("consts_ready")
        w_hi_ready = sem("w_hi_ready")
        w_lo_ready = sem("w_lo_ready")
        bn_done = sem("bn_done")
        moments = sem("moments")
        var_ready = sem("var_ready")
        rstd_done = sem("rstd_done")
        norm_ready = sem("norm_ready")
        h_ready = sem("h_ready")
        hT_ready = sem("hT_ready")
        hT_hi_ready = sem("hT_hi_ready")
        hT_split = sem("hT_split")
        qk_ready = sem("qk_ready")
        qk_drained = sem("qk_drained")
        v_ready = sem("v_ready")
        v_drained = sem("v_drained")
        x_bf_ready = sem("x_bf_ready")
        mask_ready = sem("mask_ready")
        scores_ready = sem("scores_ready")
        masked = sem("masked")
        exp_done = sem("exp_done")
        inv_ready = sem("inv_ready")
        probs_ready = sem("probs_ready")
        pT_ready = sem("pT_ready")
        pT_drained = sem("pT_drained")
        ctx_ready = sem("ctx_ready")
        cT_hi_ready = sem("cT_hi_ready")
        cT_split = sem("cT_split")
        proj_ready = sem("proj_ready")
        out_ready = sem("out_ready")

        pool_passed, dve_passed = sem("pool_passed"), sem("dve_passed")

        adj_rows = adj
        w_dram = [w.rearrange("(c p) n -> p c n", p=P) for w in (Wq, Wk, Wv, Wf)]

        def count(it, s, per=1, plus=0):
            return it * (RING * per) + (s * per + plus)

        def lap(it, s, ring=RING):
            return it * (RING // ring) + (s // ring + 1)

        def wait(eng, semaphore, value):
            if not isinstance(value, int) or value > 0:
                eng.wait_ge(semaphore, value)

        def held(eng, value):
            return value if isinstance(value, int) else eng.snap(value)

        def inside(it, s):
            return not isinstance(it, int) or 0 <= s < B

        def run(eng, step):
            for s in range(START, FIRST):
                step(0, s)
            with eng.Fori(0, LOOPS) as it:
                for s in range(FIRST, FIRST + RING):
                    step(it, s)
            for s in range(AFTER, END):
                step(0, s)

        def group_tiles(it, s):
            g = s // GROUP + 1
            if isinstance(it, int) and not 0 <= g < B // GROUP:
                return []
            return [(t, it * (2 * TILES) + (g * TILES + t)) for t in SHARE[s % GROUP]]

        def out_bank(s):
            return (ps_v, ps_qk)[len(SHARE[s % GROUP]) - 1]

        def tiles_before(it, s, place):
            s -= 1
            while len(SHARE[s % GROUP]) <= place:
                s -= 1
            g = s // GROUP + 1
            return it * (2 * TILES) + (g * TILES + SHARE[s % GROUP][place] + 1)

        block = ctx.enter_context(nc.Block())

        @block.sync
        def _(sp):
            LEAD = 11

            def at(it, s):
                return held(sp, count(it, s))

            def load_x(it, s):
                if inside(it, s):
                    here = at(it, s)
                    wait(sp, x_bf_ready, count(it, s, plus=1 - RING))
                    wait(sp, h_ready, count(it, s, plus=1 - RING))
                    sp.dma_start(x_in[:, s % RING, :], x[bass.ds(here, 1), :, :].rearrange("b p n -> (b p) n")).then_inc(x_loaded[s % RING], 16)

            def load_adj(it, s):
                if inside(it, s) and s % GROUP == 0:
                    here, made = at(it, s), held(sp, count(it, s, plus=-GROUP))
                    if not isinstance(it, int):
                        sp.wait_ge(adj_loaded[s // GROUP % 2], 16)
                    wait(sp, mask_ready, made)
                    sp.dma_start(adj_in[:, s // GROUP % 2, :, :], adj_rows[:, bass.ds(here, GROUP), :]).then_inc(adj_loaded[s // GROUP % 2], 16)

            def store(it, s):
                here = at(it, s)
                wait(sp, out_ready, count(it, s, plus=1))
                sp.dma_start(out[bass.ds(here, 1), :, :].rearrange("b p n -> (b p) n"), out_rows[:, s % O_RING, :]).then_inc(out_stored[s % O_RING], 16)

            for s in range(LEAD):
                load_x(0, s)
                if s < LEAD - GROUP:
                    load_adj(0, s)
            loops = (B - LEAD) // RING
            with sp.Fori(0, loops) as it:
                for s in range(RING):
                    store(it, s)
                    load_x(it, s + LEAD)
                    load_adj(it, s + LEAD - GROUP)
            for s in range(RING * loops, B):
                store(0, s)
                load_x(0, s + LEAD)
                load_adj(0, s + LEAD - GROUP)
            for i in range(O_RING):
                sp.wait_ge(out_stored[i], 16 * (B // O_RING))

        @block.gpsimd
        def _(pool):
            pool.memset(ident[:], 0.0).then_inc(zeroed, 1)
            pool.memset(minus_half[:], -0.5).then_inc(consts_ready, 1)
            pool.wait_ge(zeroed, 1)
            pool.affine_select(out=ident[:], in_=ident[:], compare_op=ALU.not_equal, fill=1.0, base=0,
                               pattern=[[-1, P]], channel_multiplier=1).then_inc(consts_ready, 1)
            pool.wait_ge(b_loaded, 64)
            pool.wait_ge(consts_ready, 2)

            def norm_factors(it, s):
                if not inside(it, s):
                    return
                r = s % 2
                wait(pool, h_ready, count(it, s, plus=-1))
                wait(pool, var_ready, count(it, s, plus=1))
                pool.tensor_tensor(rstd[:, r, :], var_eps[:, r, :], minus_half[:], ALU.pow).then_inc(rstd_done, 1)
                wait(pool, rstd_done, count(it, s, plus=1))
                pool.sem_inc(pool_passed)
                pool.tensor_scalar(shift[:, r, :], mean_var[:, r, 0:1], rstd[:, r, :], -1.0, ALU.mult, ALU.mult).then_inc(norm_ready, 1)

            def make_mask(it, s):
                if not inside(it, s):
                    return
                wait(pool, masked, count(it, s - 2, NH, NH))
                wait(pool, adj_loaded[s // GROUP % 2], lap(it, s) * 16)
                pool.sem_inc(pool_passed)
                pool.tensor_scalar(mask[:, s % 2, :], adj_in[:, s // GROUP % 2, s % GROUP, :], -1.0,
                                   MASKED / ROOT, ALU.add, ALU.mult).then_inc(mask_ready, 1)

            def add_bf(it, s):
                if not inside(it, s):
                    return
                wait(pool, out_ready, count(it, s, plus=1 - RING))
                wait(pool, x_loaded[s % RING], lap(it, s) * 16)
                pool.tensor_tensor(x_bf[:, s % RING, :], x_in[:, s % RING, :], bf_rows[:], ALU.add).then_inc(x_bf_ready, 1)

            def normalise(it, s):
                if not inside(it, s):
                    return
                wait(pool, pT_ready, count(it, s))
                wait(pool, inv_ready, count(it, s, plus=1))
                pool.sem_inc(pool_passed)
                for h in range(NH):
                    last = pool.tensor_scalar(probs_n[:, h, :], probs[:, h, :], inv_sum[:, h:h + 1], 1.0,
                                              ALU.mult, ALU.mult)
                last.then_inc(probs_ready, 1)

            def step(it, s):
                norm_factors(it, s + LEAD_H)
                make_mask(it, s + 1)
                add_bf(it, s + LEAD_X)
                normalise(it, s)

            run(pool, step)

        @block.scalar
        def _(act):
            act.dma_start(w_raw[:, 0, :, :], w_dram[0]).then_inc(w_loaded[0], 16)
            act.dma_start(w_raw[:, 1, :, :], w_dram[1]).then_inc(w_loaded[1], 16)
            with nc.allow_non_contiguous_dma("biases, a column for each chunk of features"):
                act.dma_start(bias_qk[:, 0:C], bq.rearrange("(c p) -> p c", p=P)).then_inc(b_loaded, 16)
                act.dma_start(bias_qk[:, C:TILES], bk.rearrange("(c p) -> p c", p=P)).then_inc(b_loaded, 16)
            act.dma_start(bv_rows[:], bv.rearrange("(a n) -> a n", a=1).broadcast_to([P, H])).then_inc(b_loaded, 16)
            act.dma_start(bf_rows[:], bf.rearrange("(a n) -> a n", a=1).broadcast_to([P, H])).then_inc(b_loaded, 16)
            act.dma_start(w_raw[:, 2, :, :], w_dram[2]).then_inc(w_loaded[2], 16)
            act.dma_start(w_raw[:, 3, :, :], w_dram[3]).then_inc(w_loaded[3], 16)
            act.wait_ge(b_loaded, 64)

            def layer_norm(it, s):
                if not inside(it, s):
                    return
                wait(act, hT_ready, count(it, s, plus=-1))
                wait(act, x_loaded[s % RING], lap(it, s) * 16)
                wait(act, norm_ready, count(it, s, plus=1))
                act.activation(h_rows[:, s % 2, :], x_in[:, s % RING, :], ACT.Relu,
                               bias=shift[:, s % 2, :], scale=rstd[:, s % 2, :]).then_inc(h_ready, 1)

            def exps(it, s):
                if not inside(it, s):
                    return
                wait(act, probs_ready, count(it, s))
                for h in range(NH):
                    wait(act, masked, count(it, s, NH, h + 1))
                    last = act.activation(probs[:, h, :], neg_scores[:, h, :], ACT.Exp,
                                          bias=neg_max[:, h:h + 1], scale=-1.0, accum_out=row_sum[:, h:h + 1])
                last.then_inc(exp_done, 1)

            def hT_to_hi(it, s):
                if not inside(it, s):
                    return
                wait(act, hT_ready, count(it, s, plus=1))
                act.activation(hT_hi[:, :, s % RING, :], ps_hT[:, 0:H].rearrange("p (c n) -> p c n", c=C),
                               ACT.Copy).then_inc(hT_hi_ready, 1)

            def drain_qk(it, s):
                for place, (t, number) in enumerate(group_tiles(it, s)):
                    wait(act, qk_ready, number + 1)
                    act.activation(qkT[:, t, (s // GROUP + 1) % 2, :], (ps_qk, ps_v)[place][:, :], ACT.Identity,
                                   bias=bias_qk[:, t:t + 1]).then_inc(qk_drained, 1)

            def drain_pT(it, s):
                if not inside(it, s):
                    return
                wait(act, pT_ready, count(it, s, plus=1))
                act.activation(pT[:, s % 2, :, :].rearrange("p (b h) n -> p b (h n)", b=2), ps_pT[:, :, 0:HALF * P],
                               ACT.Copy).then_inc(pT_drained, 1)

            def step(it, s):
                exps(it, s)
                layer_norm(it, s + LEAD_H)
                drain_qk(it, s)
                hT_to_hi(it, s + LEAD_H)
                drain_pT(it, s)
                if s == START:
                    for i in range(4):
                        act.wait_ge(w_loaded[i], 16)
                        act.activation(w_hi[:, i, :, :], w_raw[:, i, :, :], ACT.Copy).then_inc(w_hi_ready, 1)

            run(act, step)

        @block.tensor
        def _(pe):
            pe.wait_ge(consts_ready, 2)

            def three_passes(o, hi, lo, w_hi_part, w_lo_part, stationary_w=False):
                n = 0
                for c in range(C):
                    for a, w in ((hi, w_hi_part), (hi, w_lo_part), (lo, w_hi_part)):
                        lhsT, rhs = (w(c), a(c)) if stationary_w else (a(c), w(c))
                        last = pe.matmul(o, lhsT, rhs, start=(n == 0), stop=(n == 3 * C - 1))
                        n += 1
                return last

            def scores(it, s):
                if not inside(it, s):
                    return
                g = s // GROUP
                if s % GROUP == 0:
                    wait(pe, qk_drained, it * (2 * TILES) + (g + 1) * TILES)
                wait(pe, masked, count(it, s, NH))
                j = (s % GROUP) * P
                for h in range(NH):
                    rows = slice(D * (h % 2), D * (h % 2) + D)
                    bank = (ps_even, ps_odd)[h % 2]
                    last = pe.matmul(bank[:, (h // 2) * P:(h // 2 + 1) * P],
                                     qkT[rows, h // 2, g % 2, j:j + P], qkT[rows, C + h // 2, g % 2, j:j + P],
                                     start=True, stop=True)
                last.then_inc(scores_ready, 1)

            def context(it, s):
                if not inside(it, s):
                    return
                wait(pe, v_drained, count(it, s, plus=1))
                wait(pe, cT_split, count(it, s))
                wait(pe, pT_drained, count(it, s, plus=1))
                for h in range(NH):
                    o = D * (h % 2)
                    last = pe.matmul(ps_ctx[o:o + D, (h // 2) * P:(h // 2 + 1) * P],
                                     v_rows[:, s % RING, h * D:(h + 1) * D], pT[:, s % 2, h, :],
                                     start=True, stop=True)
                last.then_inc(ctx_ready, 1)

            def transpose_h(it, s):
                if not inside(it, s):
                    return
                wait(pe, hT_split, count(it, s))
                wait(pe, h_ready, count(it, s, plus=1))
                for c in range(C):
                    last = pe.transpose(ps_hT[:, c * P:(c + 1) * P], h_rows[:, s % 2, c * P:(c + 1) * P], ident[:])
                last.then_inc(hT_ready, 1)

            def project_v(it, s):
                if not inside(it, s):
                    return
                step_s = s - LEAD_V
                if isinstance(it, int) and s == 0:
                    pe.wait_ge(w_lo_ready, 3)
                wait(pe, v_drained, count(it, s))
                wait(pe, out_ready, count(it, step_s - 1))
                wait(pe, qk_drained, tiles_before(it, step_s, 1))
                wait(pe, hT_split, count(it, s, plus=1))
                r = s % RING
                three_passes(ps_v[:, 0:H], lambda c: hT_hi[:, c, r, :], lambda c: hT_lo[:, c, r, :],
                             lambda c: w_hi[:, 2, c, :], lambda c: w_lo[:, 2, c, :]).then_inc(v_ready, 1)

            def project_qk(it, s):
                g = s // GROUP + 1
                slots = slice(g % 2 * GROUP, g % 2 * GROUP + GROUP)
                for place, (t, number) in enumerate(group_tiles(it, s)):
                    if t == 0:
                        wait(pe, hT_split, count(it, g * GROUP, plus=GROUP))
                    if place:
                        wait(pe, v_drained, count(it, s + LEAD_V, plus=1))
                    else:
                        wait(pe, qk_drained, tiles_before(it, s, 0))
                    i, m = t // C, t % C
                    cols = slice(m * P, (m + 1) * P)
                    three_passes(ps_qk[:, :] if place == 0 else ps_v[:, :],
                                 lambda c: hT_hi[:, c, slots, :], lambda c: hT_lo[:, c, slots, :],
                                 lambda c: w_hi[:, i, c, cols], lambda c: w_lo[:, i, c, cols],
                                 stationary_w=True).then_inc(qk_ready, 1)

            def project_out(it, s):
                if not inside(it, s):
                    return
                if isinstance(it, int) and s == 0:
                    pe.wait_ge(w_lo_ready, 4)
                tiles = group_tiles(it, s + 1)
                if len(tiles) == 2:
                    wait(pe, qk_drained, tiles[0][1] + 1)
                elif inside(it, s + 1 + LEAD_V):
                    wait(pe, v_drained, count(it, s + 1 + LEAD_V, plus=1))
                wait(pe, out_ready, count(it, s))
                wait(pe, cT_split, count(it, s, plus=1))
                r = s % 2
                three_passes(out_bank(s + 1)[:, 0:H], lambda c: cT_hi[:, r, c, :], lambda c: cT_lo[:, r, c, :],
                             lambda c: w_hi[:, 3, c, :], lambda c: w_lo[:, 3, c, :]).then_inc(proj_ready, 1)

            def transpose_probs(it, s):
                if not inside(it, s):
                    return
                wait(pe, pT_drained, count(it, s))
                wait(pe, probs_ready, count(it, s, plus=1))
                for h in range(NH):
                    c = (h % HALF) * P
                    last = pe.transpose(ps_pT[:, h // HALF, c:c + P], probs_n[:, h, :], ident[:])
                last.then_inc(pT_ready, 1)

            def step(it, s):
                scores(it, s)
                context(it, s - 1)
                project_v(it, s + LEAD_V)
                project_qk(it, s)
                project_out(it, s - 1)
                transpose_h(it, s + LEAD_H)
                transpose_probs(it, s)

            run(pe, step)

        @block.vector
        def _(dve):
            def row_moments(it, s):
                if not inside(it, s):
                    return
                r = s % 2
                wait(dve, norm_ready, count(it, s, plus=-1))
                wait(dve, x_loaded[s % RING], lap(it, s) * 16)
                dve.bn_stats(bn[:, r, :], x_in[:, s % RING, :]).then_inc(bn_done, 1)
                wait(dve, bn_done, count(it, s, plus=1))
                dve.sem_inc(dve_passed)
                dve.bn_aggr(mean_var[:, r, :], bn[:, r, :]).then_inc(moments, 1)
                wait(dve, moments, count(it, s, plus=1))
                dve.tensor_scalar(var_eps[:, r, :], mean_var[:, r, 1:2], NORM_EPS, None, ALU.add).then_inc(var_ready, 1)

            def mask_and_max(it, s):
                if not inside(it, s):
                    return
                wait(dve, mask_ready, count(it, s, plus=1))
                wait(dve, scores_ready, count(it, s, plus=1))
                dve.sem_inc(dve_passed)
                for h in range(NH):
                    bank = (ps_even, ps_odd)[h % 2]
                    dve.tensor_tensor_reduce(neg_scores[:, h, :], bank[:, (h // 2) * P:(h // 2 + 1) * P],
                                             mask[:, s % 2, :], -ROOT, 3.0e38, ALU.add, ALU.min,
                                             neg_max[:, h:h + 1]).then_inc(masked, 1)

            def split_context(it, s):
                if not inside(it, s):
                    return
                r = s % 2
                wait(dve, ctx_ready, count(it, s, plus=1))
                dve.tensor_copy(cT_hi[:, r, :, :].rearrange("p c n -> p (c n)"), ps_ctx[:, 0:H]).then_inc(cT_hi_ready, 1)
                wait(dve, cT_hi_ready, count(it, s, plus=1))
                dve.tensor_tensor(cT_lo[:, r, :, :].rearrange("p c n -> p (c n)"), ps_ctx[:, 0:H],
                                  cT_hi[:, r, :, :].bitcast(F32).rearrange("p c n -> p (c n)"),
                                  ALU.subtract).then_inc(cT_split, 1)

            def invert_sums(it, s):
                if not inside(it, s):
                    return
                wait(dve, exp_done, count(it, s, plus=1))
                dve.reciprocal(inv_sum[:], row_sum[:]).then_inc(inv_ready, 1)

            def hT_to_lo(it, s):
                if not inside(it, s):
                    return
                wait(dve, hT_hi_ready, count(it, s, plus=1))
                dve.tensor_tensor(hT_lo[:, :, s % RING, :], ps_hT[:, 0:H].rearrange("p (c n) -> p c n", c=C),
                                  hT_hi[:, :, s % RING, :].bitcast(F32), ALU.subtract).then_inc(hT_split, 1)

            def drain_v(it, s):
                if not inside(it, s):
                    return
                wait(dve, v_ready, count(it, s, plus=1))
                dve.tensor_tensor(v_rows[:, s % RING, :], ps_v[:, 0:H], bv_rows[:], ALU.add).then_inc(v_drained, 1)

            def residual(it, s):
                if not inside(it, s):
                    return
                wait(dve, x_bf_ready, count(it, s, plus=1))
                wait(dve, out_stored[s % O_RING], (lap(it, s, O_RING) - 1) * 16)
                wait(dve, proj_ready, count(it, s, plus=1))
                dve.tensor_tensor(out_rows[:, s % O_RING, :], out_bank(s + 1)[:, 0:H], x_bf[:, s % RING, :],
                                  ALU.add).then_inc(out_ready, 1)

            def step(it, s):
                row_moments(it, s + LEAD_H)
                mask_and_max(it, s)
                split_context(it, s - 1)
                if s == START:
                    dve.wait_ge(b_loaded, 64)
                    for i in range(4):
                        dve.wait_ge(w_hi_ready, i + 1)
                        dve.tensor_tensor(w_lo[:, i, :, :], w_raw[:, i, :, :], w_hi[:, i, :, :].bitcast(F32),
                                          ALU.subtract).then_inc(w_lo_ready, 1)
                drain_v(it, s + LEAD_V)
                invert_sums(it, s)
                residual(it, s - 1)
                hT_to_lo(it, s + LEAD_H)

            run(dve, step)


_INS = ["x", "adj", "L0_gnn_Wq", "L0_gnn_bq", "L0_gnn_Wk", "L0_gnn_bk", "L0_gnn_Wv", "L0_gnn_bv", "L0_gnn_Wf", "L0_gnn_bf"]


def kernel(**inputs):
    import numpy as _np
    import concourse.bacc as _bacc
    from concourse import mybir as _mybir
    from concourse.bass_utils import run_bass_kernel_spmd as _run

    nc = _bacc.Bacc("TRN2", target_bir_lowering=False, num_devices=1)
    arrays, args = {}, []
    for name in _INS:
        a = _np.asarray(inputs[name])
        if name == "adj":
            a = a.transpose(1, 0, 2)
        a = _np.ascontiguousarray(a)
        arrays[f"in_{name}_dram"] = a
        args.append(nc.dram_tensor(f"in_{name}_dram", a.shape, _mybir.dt.from_np(a.dtype), kind="ExternalInput").ap())
    shape = inputs["x"].shape
    args.append(nc.dram_tensor("out_0_dram", shape, _mybir.dt.from_np(_np.dtype("float32")), kind="ExternalOutput").ap())
    bass_preln_graph_attention(nc, *args)
    r = _run(nc, [arrays], core_ids=[0])
    return r.results[0]["out_0_dram"]
```

```python
from contextlib import ExitStack

import concourse.bass as bass
from concourse import mybir

F32 = mybir.dt.float32
F32R = mybir.dt.float32r
U8 = mybir.dt.uint8
ALU = mybir.AluOpType
ACT = mybir.ActivationFunctionType

P = 128
RING = 8
GROUP = 4
LEAD_M = 11
LEAD_N = 9
LEAD_H = 8
LEAD_V = 1
LEAD_X = 4
NORM_EPS = 1e-5
MASKED = 9000000000000000.0


def bass_preln_graph_attention(nc, x, adj, Wq, bq, Wk, bk, Wv, bv, Wf, bf, out):
    B, S, H = x.shape
    C = H // P
    D = 64
    NH = H // D
    HALF = NH // 2
    ROOT = 0.125
    O_RING = 4
    N_RING = 4
    TILES = 2 * C
    SHARE = [[0], [1, 2], [3, 4], [5]]
    assert S == P and H == C * P and C == 3 and D * NH == H and B % RING == 0

    START, FIRST = -LEAD_M, GROUP
    LOOPS = (B - LEAD_M - FIRST) // RING
    SPLIT_AT = (START + 4, START + 7, START + 8, START + 9)
    AFTER, END = FIRST + RING * LOOPS, B + 1

    with ExitStack() as ctx:
        def sb(name, shape, dt=F32):
            return ctx.enter_context(nc.sbuf_tensor(name, shape, dt))

        def psum(name, shape):
            return ctx.enter_context(nc.psum_tensor(name, shape, F32))

        def sem(name):
            return ctx.enter_context(nc.semaphore(name))

        w_raw = sb("w_raw", [P, 4, C, H])
        w_hi = sb("w_hi", [P, 4, C, H], F32R)
        w_lo = sb("w_lo", [P, 4, C, H], F32R)
        bias_qk = sb("bias_qk", [P, TILES])
        bv_rows = sb("bv_rows", [P, H])
        bf_rows = sb("bf_rows", [P, H])
        ident = sb("ident", [P, P])
        minus_half = sb("minus_half", [P, 1])
        table_probe = sb("table_probe", [P, 1])
        x_in = sb("x_in", [P, RING, H])
        x_bf = sb("x_bf", [P, RING, H])
        h_rows = sb("h_rows", [P, 2, H])
        hT_hi = sb("hT_hi", [P, C, RING, P], F32R)
        hT_lo = sb("hT_lo", [P, C, RING, P], F32R)
        qkT = sb("qkT", [P, TILES, 2, GROUP * P])
        v_rows = sb("v_rows", [P, RING, H])
        adj_in = sb("adj_in", [P, 2, GROUP, P], U8)
        mask = sb("mask", [P, 2, P])
        neg_scores = sb("neg_scores", [P, NH, P])
        neg_max = sb("neg_max", [P, NH])
        probs = sb("probs", [P, NH, P])
        row_sum = sb("row_sum", [P, NH])
        inv_sum = sb("inv_sum", [P, NH])
        probs_n = sb("probs_n", [P, NH, P])
        pT = sb("pT", [P, 2, NH, P])
        cT_hi = sb("cT_hi", [P, 2, C, P], F32R)
        cT_lo = sb("cT_lo", [P, 2, C, P], F32R)
        out_rows = sb("out_rows", [P, O_RING, H])
        bn = sb("bn", [P, N_RING, 6])
        mean_var = sb("mean_var", [P, N_RING, 2])
        var_eps = sb("var_eps", [P, N_RING, 1])
        rstd = sb("rstd", [P, N_RING, 1])
        shift = sb("shift", [P, N_RING, 1])

        ps_even = psum("ps_even", [P, 512])
        ps_odd = psum("ps_odd", [P, 512])
        ps_pT = psum("ps_pT", [P, 2, 512])
        ps_ctx = psum("ps_ctx", [P, 512])
        ps_hT = psum("ps_hT", [P, 512])
        ps_v = psum("ps_v", [P, 512])
        ps_qk = psum("ps_qk", [P, 512])

        w_loaded = [sem(f"w_loaded{i}") for i in range(4)]
        b_loaded = sem("b_loaded")
        x_loaded = [sem(f"x_loaded{i}") for i in range(RING)]
        adj_loaded = [sem(f"adj_loaded{i}") for i in range(2)]
        out_stored = [sem(f"out_stored{i}") for i in range(O_RING)]
        zeroed = sem("zeroed")
        consts_ready = sem("consts_ready")
        w_hi_ready = sem("w_hi_ready")
        w_lo_ready = sem("w_lo_ready")
        bn_done = sem("bn_done")
        moments = sem("moments")
        var_ready = sem("var_ready")
        rstd_done = sem("rstd_done")
        norm_ready = sem("norm_ready")
        h_ready = sem("h_ready")
        hT_ready = sem("hT_ready")
        hT_hi_ready = sem("hT_hi_ready")
        hT_split = sem("hT_split")
        qk_ready = sem("qk_ready")
        qk_drained = sem("qk_drained")
        v_ready = sem("v_ready")
        v_drained = sem("v_drained")
        x_bf_ready = sem("x_bf_ready")
        mask_ready = sem("mask_ready")
        scores_ready = sem("scores_ready")
        masked = sem("masked")
        exp_done = sem("exp_done")
        inv_ready = sem("inv_ready")
        probs_ready = sem("probs_ready")
        pT_ready = sem("pT_ready")
        pT_drained = sem("pT_drained")
        ctx_ready = sem("ctx_ready")
        cT_hi_ready = sem("cT_hi_ready")
        cT_split = sem("cT_split")
        proj_ready = sem("proj_ready")
        out_ready = sem("out_ready")

        pool_passed, dve_passed = sem("pool_passed"), sem("dve_passed")

        adj_rows = adj
        W_Q, W_K, W_V, W_F = range(4)
        w_dram = [w.rearrange("(c p) n -> p c n", p=P) for w in (Wq, Wk, Wv, Wf)]

        def count(it, s, per=1, plus=0):
            return it * (RING * per) + (s * per + plus)

        def lap(it, s, ring=RING):
            return it * (RING // ring) + (s // ring + 1)

        def wait(eng, semaphore, value):
            if not isinstance(value, int) or value > 0:
                eng.wait_ge(semaphore, value)

        def held(eng, value):
            return value if isinstance(value, int) else eng.snap(value)

        def inside(it, s):
            return not isinstance(it, int) or 0 <= s < B

        def run(eng, step):
            for s in range(START, FIRST):
                step(0, s)
            with eng.Fori(0, LOOPS) as it:
                for s in range(FIRST, FIRST + RING):
                    step(it, s)
            for s in range(AFTER, END):
                step(0, s)

        def group_tiles(it, s):
            g = s // GROUP + 1
            if isinstance(it, int) and not 0 <= g < B // GROUP:
                return []
            return [(t, it * (2 * TILES) + (g * TILES + t)) for t in SHARE[s % GROUP]]

        def hT_bank(it, s):
            return ps_ctx if isinstance(it, int) and s < LEAD_H and s % 2 else ps_hT

        def second_bank(it, s):
            return ps_odd if isinstance(it, int) and s < 0 else ps_v

        def out_bank(s):
            return (ps_v, ps_qk)[len(SHARE[s % GROUP]) - 1]

        def tiles_before(it, s, place):
            s -= 1
            while len(SHARE[s % GROUP]) <= place:
                s -= 1
            made = s // GROUP * TILES + TILES + SHARE[s % GROUP][place] + 1
            if isinstance(it, int):
                return min(made, B // GROUP * TILES)
            return it * (2 * TILES) + made

        block = ctx.enter_context(nc.Block())

        @block.sync
        def _(sp):
            LEAD = 13
            LEAD_ADJ = 2 * GROUP

            def at(it, s):
                return held(sp, count(it, s))

            def load_x(it, s):
                if inside(it, s):
                    here = at(it, s)
                    wait(sp, x_bf_ready, count(it, s, plus=1 - RING))
                    wait(sp, h_ready, count(it, s, plus=1 - RING))
                    sp.dma_start(x_in[:, s % RING, :], x[bass.ds(here, 1), :, :].rearrange("b p n -> (b p) n")).then_inc(x_loaded[s % RING], 16)

            def load_adj(it, s):
                if inside(it, s) and s % GROUP == 0:
                    here, made = at(it, s), held(sp, count(it, s, plus=-GROUP))
                    if not isinstance(it, int):
                        sp.wait_ge(adj_loaded[s // GROUP % 2], 16)
                    wait(sp, mask_ready, made)
                    sp.dma_start(adj_in[:, s // GROUP % 2, :, :], adj_rows[:, bass.ds(here, GROUP), :]).then_inc(adj_loaded[s // GROUP % 2], 16)

            def load_w(i):
                sp.dma_start(w_raw[:, i, :, :], w_dram[i]).then_inc(w_loaded[i], 16)

            def store(it, s):
                here = at(it, s)
                wait(sp, out_ready, count(it, s, plus=1))
                sp.dma_start(out[bass.ds(here, 1), :, :].rearrange("b p n -> (b p) n"), out_rows[:, s % O_RING, :]).then_inc(out_stored[s % O_RING], 16)

            for s in range(GROUP):
                load_x(0, s)
            load_w(W_Q)
            load_x(0, GROUP)
            load_x(0, GROUP + 1)
            load_w(W_K)
            with nc.allow_non_contiguous_dma("biases, a column for each chunk of features"):
                sp.dma_start(bias_qk[:, 0:C], bq.rearrange("(c p) -> p c", p=P)).then_inc(b_loaded, 16)
                sp.dma_start(bias_qk[:, C:TILES], bk.rearrange("(c p) -> p c", p=P)).then_inc(b_loaded, 16)
            load_w(W_V)
            sp.dma_start(bv_rows[:], bv.rearrange("(a n) -> a n", a=1).broadcast_to([P, H])).then_inc(b_loaded, 16)
            sp.dma_start(bf_rows[:], bf.rearrange("(a n) -> a n", a=1).broadcast_to([P, H])).then_inc(b_loaded, 16)
            for s in range(GROUP + 2, RING):
                load_x(0, s)
            load_w(W_F)
            for s in range(LEAD_ADJ):
                load_adj(0, s)
            for s in range(RING, LEAD):
                load_x(0, s)
            loops = (B - LEAD) // RING
            with sp.Fori(0, loops) as it:
                for s in range(RING):
                    store(it, s)
                    load_x(it, s + LEAD)
                    load_adj(it, s + LEAD_ADJ)
            for s in range(RING * loops, B):
                store(0, s)
                load_x(0, s + LEAD)
                load_adj(0, s + LEAD_ADJ)
            for i in range(O_RING):
                sp.wait_ge(out_stored[i], 16 * (B // O_RING))

        @block.gpsimd
        def _(pool):
            pool.memset(ident[:], 0.0).then_inc(zeroed, 1)
            pool.memset(minus_half[:], -0.5).then_inc(consts_ready, 1)
            pool.wait_ge(zeroed, 1)
            pool.affine_select(out=ident[:], in_=ident[:], compare_op=ALU.not_equal, fill=1.0, base=0,
                               pattern=[[-1, P]], channel_multiplier=1).then_inc(consts_ready, 1)
            pool.wait_ge(consts_ready, 2)

            def norm_factors(it, s):
                if not inside(it, s):
                    return
                r = s % N_RING
                wait(pool, h_ready, count(it, s, plus=1 - N_RING))
                wait(pool, var_ready, count(it, s, plus=1))
                pool.tensor_tensor(rstd[:, r, :], var_eps[:, r, :], minus_half[:], ALU.pow).then_inc(rstd_done, 1)
                wait(pool, rstd_done, count(it, s, plus=1))
                pool.sem_inc(pool_passed)
                pool.tensor_scalar(shift[:, r, :], mean_var[:, r, 0:1], rstd[:, r, :], -1.0, ALU.mult, ALU.mult).then_inc(norm_ready, 1)

            def make_mask(it, s):
                if not inside(it, s):
                    return
                wait(pool, masked, count(it, s - 2, NH, NH))
                wait(pool, adj_loaded[s // GROUP % 2], lap(it, s) * 16)
                pool.sem_inc(pool_passed)
                pool.tensor_scalar(mask[:, s % 2, :], adj_in[:, s // GROUP % 2, s % GROUP, :], -1.0,
                                   MASKED / ROOT, ALU.add, ALU.mult).then_inc(mask_ready, 1)

            def add_bf(it, s):
                if not inside(it, s):
                    return
                if isinstance(it, int) and s == 0:
                    pool.wait_ge(b_loaded, 64)
                wait(pool, out_ready, count(it, s, plus=1 - RING))
                wait(pool, x_loaded[s % RING], lap(it, s) * 16)
                pool.tensor_tensor(x_bf[:, s % RING, :], x_in[:, s % RING, :], bf_rows[:], ALU.add).then_inc(x_bf_ready, 1)

            def normalise(it, s):
                if not inside(it, s):
                    return
                wait(pool, pT_ready, count(it, s))
                wait(pool, inv_ready, count(it, s, plus=1))
                pool.sem_inc(pool_passed)
                for h in range(NH):
                    last = pool.tensor_scalar(probs_n[:, h, :], probs[:, h, :], inv_sum[:, h:h + 1], 1.0,
                                              ALU.mult, ALU.mult)
                last.then_inc(probs_ready, 1)

            def step(it, s):
                make_mask(it, s + 1)
                add_bf(it, s + LEAD_X)
                normalise(it, s)
                norm_factors(it, s + LEAD_M)

            run(pool, step)

        @block.scalar
        def _(act):
            act.wait_ge(consts_ready, 2)
            act.activation(table_probe[:], minus_half[:], ACT.Exp)

            def layer_norm(it, s):
                if not inside(it, s):
                    return
                wait(act, hT_ready, count(it, s, plus=-1))
                wait(act, x_loaded[s % RING], lap(it, s) * 16)
                wait(act, norm_ready, count(it, s, plus=1))
                act.activation(h_rows[:, s % 2, :], x_in[:, s % RING, :], ACT.Relu,
                               bias=shift[:, s % N_RING, :], scale=rstd[:, s % N_RING, :]).then_inc(h_ready, 1)

            def exps(it, s):
                if not inside(it, s):
                    return
                wait(act, probs_ready, count(it, s))
                for h in range(NH):
                    wait(act, masked, count(it, s, NH, h + 1))
                    last = act.activation(probs[:, h, :], neg_scores[:, h, :], ACT.Exp,
                                          bias=neg_max[:, h:h + 1], scale=-1.0, accum_out=row_sum[:, h:h + 1])
                last.then_inc(exp_done, 1)

            def hT_to_hi(it, s):
                if not inside(it, s):
                    return
                wait(act, hT_ready, count(it, s, plus=1))
                act.activation(hT_hi[:, :, s % RING, :], hT_bank(it, s)[:, 0:H].rearrange("p (c n) -> p c n", c=C),
                               ACT.Copy).then_inc(hT_hi_ready, 1)

            def drain_qk(it, s):
                for place, (t, number) in enumerate(group_tiles(it, s)):
                    if isinstance(it, int) and number == 0:
                        act.wait_ge(b_loaded, 64)
                    wait(act, qk_ready, number + 1)
                    act.activation(qkT[:, t, (s // GROUP + 1) % 2, :], (ps_qk, second_bank(it, s))[place][:, :], ACT.Identity,
                                   bias=bias_qk[:, t:t + 1]).then_inc(qk_drained, 1)

            def drain_pT(it, s):
                if not inside(it, s):
                    return
                wait(act, pT_ready, count(it, s, plus=1))
                act.activation(pT[:, s % 2, :, :].rearrange("p (b h) n -> p b (h n)", b=2), ps_pT[:, :, 0:HALF * P],
                               ACT.Copy).then_inc(pT_drained, 1)

            def step(it, s):
                exps(it, s)
                layer_norm(it, s + LEAD_N)
                drain_qk(it, s)
                hT_to_hi(it, s + LEAD_H)
                drain_pT(it, s)
                if isinstance(it, int) and s in SPLIT_AT:
                    i = SPLIT_AT.index(s)
                    act.wait_ge(w_loaded[i], 16)
                    act.activation(w_hi[:, i, :, :], w_raw[:, i, :, :], ACT.Copy).then_inc(w_hi_ready, 1)

            run(act, step)

        @block.tensor
        def _(pe):
            pe.wait_ge(consts_ready, 2)

            def three_passes(o, hi, lo, w_hi_part, w_lo_part, stationary_w=False):
                n = 0
                for c in range(C):
                    for a, w in ((hi, w_hi_part), (hi, w_lo_part), (lo, w_hi_part)):
                        lhsT, rhs = (w(c), a(c)) if stationary_w else (a(c), w(c))
                        last = pe.matmul(o, lhsT, rhs, start=(n == 0), stop=(n == 3 * C - 1))
                        n += 1
                return last

            def scores(it, s):
                if not inside(it, s):
                    return
                g = s // GROUP
                if s % GROUP == 0:
                    wait(pe, qk_drained, it * (2 * TILES) + (g + 1) * TILES)
                wait(pe, masked, count(it, s, NH))
                j = (s % GROUP) * P
                for h in range(NH):
                    rows = slice(D * (h % 2), D * (h % 2) + D)
                    bank = (ps_even, ps_odd)[h % 2]
                    last = pe.matmul(bank[:, (h // 2) * P:(h // 2 + 1) * P],
                                     qkT[rows, h // 2, g % 2, j:j + P], qkT[rows, C + h // 2, g % 2, j:j + P],
                                     start=True, stop=True)
                last.then_inc(scores_ready, 1)

            def context(it, s):
                if not inside(it, s):
                    return
                wait(pe, v_drained, count(it, s, plus=1))
                wait(pe, cT_split, count(it, s))
                wait(pe, pT_drained, count(it, s, plus=1))
                for h in range(NH):
                    o = D * (h % 2)
                    last = pe.matmul(ps_ctx[o:o + D, (h // 2) * P:(h // 2 + 1) * P],
                                     v_rows[:, s % RING, h * D:(h + 1) * D], pT[:, s % 2, h, :],
                                     start=True, stop=True)
                last.then_inc(ctx_ready, 1)

            def transpose_h(it, s):
                if not inside(it, s):
                    return
                wait(pe, hT_split, count(it, s - (isinstance(it, int) and s < LEAD_H)))
                wait(pe, h_ready, count(it, s, plus=1))
                for c in range(C):
                    last = pe.transpose(hT_bank(it, s)[:, c * P:(c + 1) * P], h_rows[:, s % 2, c * P:(c + 1) * P], ident[:])
                last.then_inc(hT_ready, 1)

            def project_v(it, s):
                if not inside(it, s):
                    return
                step_s = s - LEAD_V
                if isinstance(it, int) and s == 0:
                    pe.wait_ge(w_lo_ready, W_V + 1)
                wait(pe, v_drained, count(it, s))
                wait(pe, out_ready, count(it, step_s - 1))
                if not isinstance(it, int) or step_s > 1:
                    wait(pe, qk_drained, tiles_before(it, step_s, 1))
                wait(pe, hT_split, count(it, s, plus=1))
                r = s % RING
                three_passes(ps_v[:, 0:H], lambda c: hT_hi[:, c, r, :], lambda c: hT_lo[:, c, r, :],
                             lambda c: w_hi[:, W_V, c, :], lambda c: w_lo[:, W_V, c, :]).then_inc(v_ready, 1)

            def project_qk(it, s):
                g = s // GROUP + 1
                slots = slice(g % 2 * GROUP, g % 2 * GROUP + GROUP)
                for place, (t, number) in enumerate(group_tiles(it, s)):
                    if t == 0:
                        wait(pe, hT_split, count(it, g * GROUP, plus=GROUP))
                    if place and second_bank(it, s) is ps_v:
                        wait(pe, v_drained, count(it, s + LEAD_V, plus=1))
                    elif place:
                        wait(pe, qk_drained, tiles_before(it, s, 1))
                    else:
                        wait(pe, qk_drained, tiles_before(it, s, 0))
                    i, m = (W_Q, W_K)[t // C], t % C
                    if isinstance(it, int) and g == 0:
                        pe.wait_ge(w_lo_ready, i + 1)
                    cols = slice(m * P, (m + 1) * P)
                    three_passes((ps_qk, second_bank(it, s))[place][:, :],
                                 lambda c: hT_hi[:, c, slots, :], lambda c: hT_lo[:, c, slots, :],
                                 lambda c: w_hi[:, i, c, cols], lambda c: w_lo[:, i, c, cols],
                                 stationary_w=True).then_inc(qk_ready, 1)

            def project_out(it, s):
                if not inside(it, s):
                    return
                if isinstance(it, int) and s == 0:
                    pe.wait_ge(w_lo_ready, W_F + 1)
                tiles = group_tiles(it, s + 1)
                if len(tiles) == 2:
                    wait(pe, qk_drained, tiles[0][1] + 1)
                elif inside(it, s + 1 + LEAD_V):
                    wait(pe, v_drained, count(it, s + 1 + LEAD_V, plus=1))
                wait(pe, out_ready, count(it, s))
                wait(pe, cT_split, count(it, s, plus=1))
                r = s % 2
                three_passes(out_bank(s + 1)[:, 0:H], lambda c: cT_hi[:, r, c, :], lambda c: cT_lo[:, r, c, :],
                             lambda c: w_hi[:, W_F, c, :], lambda c: w_lo[:, W_F, c, :]).then_inc(proj_ready, 1)

            def transpose_probs(it, s):
                if not inside(it, s):
                    return
                wait(pe, pT_drained, count(it, s))
                wait(pe, probs_ready, count(it, s, plus=1))
                for h in range(NH):
                    c = (h % HALF) * P
                    last = pe.transpose(ps_pT[:, h // HALF, c:c + P], probs_n[:, h, :], ident[:])
                last.then_inc(pT_ready, 1)

            def step(it, s):
                project_v(it, s + LEAD_V)
                context(it, s - 1)
                project_qk(it, s)
                filled = len(group_tiles(it, s)) > 0
                if not filled:
                    scores(it, s + 1)
                project_out(it, s - 1)
                transpose_h(it, s + LEAD_H)
                if filled:
                    scores(it, s + 1)
                transpose_probs(it, s)

            run(pe, step)

        @block.vector
        def _(dve):
            def row_moments(it, s):
                if not inside(it, s):
                    return
                r = s % N_RING
                wait(dve, norm_ready, count(it, s, plus=1 - N_RING))
                wait(dve, x_loaded[s % RING], lap(it, s) * 16)
                dve.bn_stats(bn[:, r, :], x_in[:, s % RING, :]).then_inc(bn_done, 1)
                wait(dve, bn_done, count(it, s, plus=1))
                dve.sem_inc(dve_passed)
                dve.bn_aggr(mean_var[:, r, :], bn[:, r, :]).then_inc(moments, 1)
                wait(dve, moments, count(it, s, plus=1))
                dve.tensor_scalar(var_eps[:, r, :], mean_var[:, r, 1:2], NORM_EPS, None, ALU.add).then_inc(var_ready, 1)

            def mask_and_max(it, s):
                if not inside(it, s):
                    return
                wait(dve, mask_ready, count(it, s, plus=1))
                wait(dve, scores_ready, count(it, s, plus=1))
                dve.sem_inc(dve_passed)
                for h in range(NH):
                    bank = (ps_even, ps_odd)[h % 2]
                    dve.tensor_tensor_reduce(neg_scores[:, h, :], bank[:, (h // 2) * P:(h // 2 + 1) * P],
                                             mask[:, s % 2, :], -ROOT, 3.0e38, ALU.add, ALU.min,
                                             neg_max[:, h:h + 1]).then_inc(masked, 1)

            def split_context(it, s):
                if not inside(it, s):
                    return
                r = s % 2
                wait(dve, ctx_ready, count(it, s, plus=1))
                dve.tensor_copy(cT_hi[:, r, :, :].rearrange("p c n -> p (c n)"), ps_ctx[:, 0:H]).then_inc(cT_hi_ready, 1)
                wait(dve, cT_hi_ready, count(it, s, plus=1))
                dve.tensor_tensor(cT_lo[:, r, :, :].rearrange("p c n -> p (c n)"), ps_ctx[:, 0:H],
                                  cT_hi[:, r, :, :].bitcast(F32).rearrange("p c n -> p (c n)"),
                                  ALU.subtract).then_inc(cT_split, 1)

            def invert_sums(it, s):
                if not inside(it, s):
                    return
                wait(dve, exp_done, count(it, s, plus=1))
                dve.reciprocal(inv_sum[:], row_sum[:]).then_inc(inv_ready, 1)

            def hT_to_lo(it, s):
                if not inside(it, s):
                    return
                wait(dve, hT_hi_ready, count(it, s, plus=1))
                dve.tensor_tensor(hT_lo[:, :, s % RING, :], hT_bank(it, s)[:, 0:H].rearrange("p (c n) -> p c n", c=C),
                                  hT_hi[:, :, s % RING, :].bitcast(F32), ALU.subtract).then_inc(hT_split, 1)

            def drain_v(it, s):
                if not inside(it, s):
                    return
                if isinstance(it, int) and s == 0:
                    dve.wait_ge(b_loaded, 64)
                wait(dve, v_ready, count(it, s, plus=1))
                dve.tensor_tensor(v_rows[:, s % RING, :], ps_v[:, 0:H], bv_rows[:], ALU.add).then_inc(v_drained, 1)

            def residual(it, s):
                if not inside(it, s):
                    return
                wait(dve, x_bf_ready, count(it, s, plus=1))
                wait(dve, out_stored[s % O_RING], (lap(it, s, O_RING) - 1) * 16)
                wait(dve, proj_ready, count(it, s, plus=1))
                dve.tensor_tensor(out_rows[:, s % O_RING, :], out_bank(s + 1)[:, 0:H], x_bf[:, s % RING, :],
                                  ALU.add).then_inc(out_ready, 1)

            def step(it, s):
                drain_v(it, s + LEAD_V)
                split_context(it, s - 1)
                invert_sums(it, s)
                residual(it, s - 1)
                hT_to_lo(it, s + LEAD_H)
                row_moments(it, s + LEAD_M)
                mask_and_max(it, s + 1)
                if isinstance(it, int) and s in SPLIT_AT:
                    i = SPLIT_AT.index(s)
                    dve.wait_ge(w_hi_ready, i + 1)
                    dve.tensor_tensor(w_lo[:, i, :, :], w_raw[:, i, :, :], w_hi[:, i, :, :].bitcast(F32),
                                      ALU.subtract).then_inc(w_lo_ready, 1)

            run(dve, step)


_INS = ["x", "adj", "L0_gnn_Wq", "L0_gnn_bq", "L0_gnn_Wk", "L0_gnn_bk", "L0_gnn_Wv", "L0_gnn_bv", "L0_gnn_Wf", "L0_gnn_bf"]


def kernel(**inputs):
    import numpy as _np
    import concourse.bacc as _bacc
    from concourse import mybir as _mybir
    from concourse.bass_utils import run_bass_kernel_spmd as _run

    nc = _bacc.Bacc("TRN2", target_bir_lowering=False, num_devices=1)
    arrays, args = {}, []
    for name in _INS:
        a = _np.asarray(inputs[name])
        if name == "adj":
            a = a.transpose(1, 0, 2)
        a = _np.ascontiguousarray(a)
        arrays[f"in_{name}_dram"] = a
        args.append(nc.dram_tensor(f"in_{name}_dram", a.shape, _mybir.dt.from_np(a.dtype), kind="ExternalInput").ap())
    shape = inputs["x"].shape
    args.append(nc.dram_tensor("out_0_dram", shape, _mybir.dt.from_np(_np.dtype("float32")), kind="ExternalOutput").ap())
    bass_preln_graph_attention(nc, *args)
    r = _run(nc, [arrays], core_ids=[0])
    return r.results[0]["out_0_dram"]
```

```python
from contextlib import ExitStack

import concourse.bass as bass
from concourse import mybir

F32 = mybir.dt.float32
F32R = mybir.dt.float32r
U8 = mybir.dt.uint8
ALU = mybir.AluOpType
ACT = mybir.ActivationFunctionType

P = 128
RING = 8
GROUP = 4
LEAD_M = 11
LEAD_N = 9
LEAD_H = 8
LEAD_V = 1
LEAD_X = 4
NORM_EPS = 1e-5
MASKED = 9000000000000000.0


def bass_preln_graph_attention(nc, x, adj, Wq, bq, Wk, bk, Wv, bv, Wf, bf, out):
    B, S, H = x.shape
    C = H // P
    D = 64
    NH = H // D
    HALF = NH // 2
    ROOT = 0.125
    O_RING = 4
    V_RING = 4
    N_RING = 4
    TILES = 2 * C
    SHARE = [[0], [1, 2], [3, 4], [5]]
    TILE = [(0, 0), (0, 1), (1, 0), (0, 2), (1, 1), (1, 2)]
    HI_STEPS = sum(1 + kind for kind, _ in TILE)
    assert S == P and H == C * P and C == 3 and D * NH == H and B % RING == 0

    START, FIRST = -LEAD_M, GROUP
    LOOPS = (B - LEAD_M - FIRST) // RING
    SPLIT_AT = (START + 5, START + 6, START + 7, START + 10)
    ZERO_AT = START + 7
    AFTER, END = FIRST + RING * LOOPS, B + 1

    with ExitStack() as ctx:
        def sb(name, shape, dt=F32):
            return ctx.enter_context(nc.sbuf_tensor(name, shape, dt))

        def psum(name, shape):
            return ctx.enter_context(nc.psum_tensor(name, shape, F32))

        def sem(name):
            return ctx.enter_context(nc.semaphore(name))

        w_hi = sb("w_hi", [P, 4, C, H], F32R)
        w_lo = sb("w_lo", [P, 4, C, H], F32R)
        bias_qk = sb("bias_qk", [P, TILES])
        bv_rows = sb("bv_rows", [P, H])
        bf_rows = sb("bf_rows", [P, H])
        ident = sb("ident", [P, P])
        minus_half = sb("minus_half", [P, 1])
        table_probe = sb("table_probe", [P, 1])
        x_in = sb("x_in", [P, RING, H])
        x_bf = sb("x_bf", [P, RING, H])
        h_rows = sb("h_rows", [P, 2, H])
        hT_hi = sb("hT_hi", [P, C, RING, P], F32R)
        hT_lo = sb("hT_lo", [P, C, RING, P], F32R)
        HI, LO = range(2)
        q_parts = sb("q_parts", [P, 2, C, 2, GROUP * P], F32R)
        k_parts = sb("k_parts", [P, 2, 2, C, GROUP, 2, P], F32R)
        adj_in = sb("adj_in", [P, 2, GROUP, P], U8)
        mask = sb("mask", [P, 2, P])
        neg_max = sb("neg_max", [P, NH])
        row_sum = sb("row_sum", [P, NH])
        inv_sum = sb("inv_sum", [P, NH])
        pieces = (V_RING * H, NH * P, NH * P, NH * P, 2 * NH * P)
        shared = sb("shared", [P, sum(pieces)])
        w_raw = shared[:, 0:4 * C * H].rearrange("p (w c n) -> p w c n", w=4, c=C)
        views = [shared[:, sum(pieces[:i]):sum(pieces[:i + 1])] for i in range(5)]
        v_rows = views[0].rearrange("p (r n) -> p r n", r=V_RING)
        neg_scores, probs, probs_n = [v.rearrange("p (h n) -> p h n", h=NH) for v in views[1:4]]
        pT = views[4].rearrange("p (r h n) -> p r h n", r=2, h=NH)
        cT_hi = sb("cT_hi", [P, 2, C, P], F32R)
        cT_lo = sb("cT_lo", [P, 2, C, P], F32R)
        out_rows = sb("out_rows", [P, O_RING, H])
        bn = sb("bn", [P, N_RING, 6])
        mean_var = sb("mean_var", [P, N_RING, 2])
        var_eps = sb("var_eps", [P, N_RING, 1])
        rstd = sb("rstd", [P, N_RING, 1])
        shift = sb("shift", [P, N_RING, 1])

        ps_sc = [psum(f"ps_sc{i}", [P, 512]) for i in range(2)]
        ps_pT = psum("ps_pT", [P, 2, 512])
        ps_ctx = psum("ps_ctx", [P, 512])
        ps_hT = psum("ps_hT", [P, 512])
        ps_v = psum("ps_v", [P, 512])
        ps_qk = psum("ps_qk", [P, 512])

        w_loaded = [sem(f"w_loaded{i}") for i in range(4)]
        b_loaded = sem("b_loaded")
        x_loaded = [sem(f"x_loaded{i}") for i in range(RING)]
        adj_loaded = [sem(f"adj_loaded{i}") for i in range(2)]
        out_stored = [sem(f"out_stored{i}") for i in range(O_RING)]
        zeroed = sem("zeroed")
        consts_ready = sem("consts_ready")
        w_hi_ready = sem("w_hi_ready")
        w_lo_ready = sem("w_lo_ready")
        bn_done = sem("bn_done")
        moments = sem("moments")
        var_ready = sem("var_ready")
        rstd_done = sem("rstd_done")
        norm_ready = sem("norm_ready")
        h_ready = sem("h_ready")
        hT_ready = sem("hT_ready")
        hT_hi_ready = sem("hT_hi_ready")
        hT_split = sem("hT_split")
        qk_ready = sem("qk_ready")
        qk_hi_ready = sem("qk_hi_ready")
        qk_drained = sem("qk_drained")
        k_zeroed = sem("k_zeroed")
        v_ready = sem("v_ready")
        v_drained = sem("v_drained")
        x_bf_ready = sem("x_bf_ready")
        mask_ready = sem("mask_ready")
        scores_ready = sem("scores_ready")
        masked = sem("masked")
        exp_done = sem("exp_done")
        inv_ready = sem("inv_ready")
        probs_ready = sem("probs_ready")
        pT_ready = sem("pT_ready")
        pT_drained = sem("pT_drained")
        ctx_ready = sem("ctx_ready")
        cT_hi_ready = sem("cT_hi_ready")
        cT_split = sem("cT_split")
        proj_ready = sem("proj_ready")
        out_ready = sem("out_ready")

        pool_passed, dve_passed = sem("pool_passed"), sem("dve_passed")

        adj_rows = adj
        W_Q, W_K, W_V, W_F = range(4)
        w_dram = [w.rearrange("(c p) n -> p c n", p=P) for w in (Wq, Wk, Wv, Wf)]

        def count(it, s, per=1, plus=0):
            return it * (RING * per) + (s * per + plus)

        def lap(it, s, ring=RING):
            return it * (RING // ring) + (s // ring + 1)

        def wait(eng, semaphore, value):
            if not isinstance(value, int) or value > 0:
                eng.wait_ge(semaphore, value)

        def held(eng, value):
            return value if isinstance(value, int) else eng.snap(value)

        def inside(it, s):
            return not isinstance(it, int) or 0 <= s < B

        def run(eng, step):
            for s in range(START, FIRST):
                step(0, s)
            with eng.Fori(0, LOOPS) as it:
                for s in range(FIRST, FIRST + RING):
                    step(it, s)
            for s in range(AFTER, END):
                step(0, s)

        def group_tiles(it, s):
            g = s // GROUP + 1
            if isinstance(it, int) and not 0 <= g < B // GROUP:
                return []
            return [(t, it * (2 * TILES) + (g * TILES + t)) for t in SHARE[s % GROUP]]

        def hT_bank(it, s):
            return ps_ctx if isinstance(it, int) and s < LEAD_H and s % 2 else ps_hT

        def filled(it, s):
            return len(group_tiles(it, s)) > 0

        def tile_bank(it, s, place):
            if isinstance(it, int) and s == -3:
                return ps_sc[place]
            if isinstance(it, int) and s == -2:
                return ps_pT[:, place, :]
            return (ps_qk, ps_v)[place]

        def k_rows(e):
            return slice(e * D, e * D + D)

        def k_zeros(group, e):
            return k_parts[k_rows(e), group % 2, :, :, :, 1 - e, :].rearrange("p a c j n -> p (a c j) n")

        def zero_k(eng, group, e):
            to = k_zeros(group, e)
            ones_and_zeros = ident[k_rows(e), None, :].broadcast_to([D, to.shape[1], P])
            if e == 0:
                eng.tensor_scalar(to, ones_and_zeros, 0.0, None, ALU.mult).then_inc(k_zeroed, 1)
            else:
                eng.activation(to, ones_and_zeros, ACT.Copy, scale=0.0).then_inc(k_zeroed, 1)

        def tile_parts(it, s, t, part):
            kind, c = TILE[t]
            par = (s // GROUP + 1) % 2
            if kind == 0:
                return [(slice(0, P), q_parts[:, part, c, par, :].rearrange("p (j n) -> p j n", j=GROUP))]
            return [(k_rows(e), k_parts[k_rows(e), par, part, c, :, e, :]) for e in range(2)]

        def hi_count(it, s, t, n):
            return it * (2 * HI_STEPS) + ((s // GROUP + 1) * HI_STEPS + sum(1 + kind for kind, _ in TILE[:t]) + n)

        def head_scores(h):
            return ps_sc[h // 4][:, h % 4 * P:h % 4 * P + P]

        def out_bank(s):
            return ps_v if len(SHARE[s % GROUP]) == 1 and s < B - GROUP else ps_qk

        def tiles_before(it, s, place):
            s -= 1
            while len(SHARE[s % GROUP]) <= place:
                s -= 1
            made = s // GROUP * TILES + TILES + SHARE[s % GROUP][place] + 1
            if isinstance(it, int):
                return min(made, B // GROUP * TILES)
            return it * (2 * TILES) + made

        block = ctx.enter_context(nc.Block())

        @block.sync
        def _(sp):
            LEAD = 13
            LEAD_ADJ = 2 * GROUP

            def at(it, s):
                return held(sp, count(it, s))

            def load_x(it, s):
                if inside(it, s):
                    here = at(it, s)
                    wait(sp, x_bf_ready, count(it, s, plus=1 - RING))
                    wait(sp, h_ready, count(it, s, plus=1 - RING))
                    sp.dma_start(x_in[:, s % RING, :], x[bass.ds(here, 1), :, :].rearrange("b p n -> (b p) n")).then_inc(x_loaded[s % RING], 16)

            def load_adj(it, s):
                if inside(it, s) and s % GROUP == 0:
                    here, made = at(it, s), held(sp, count(it, s, plus=-GROUP))
                    if not isinstance(it, int):
                        sp.wait_ge(adj_loaded[s // GROUP % 2], 16)
                    wait(sp, mask_ready, made)
                    sp.dma_start(adj_in[:, s // GROUP % 2, :, :], adj_rows[:, bass.ds(here, GROUP), :]).then_inc(adj_loaded[s // GROUP % 2], 16)

            def load_w(i):
                sp.dma_start(w_raw[:, i, :, :], w_dram[i]).then_inc(w_loaded[i], 16)

            def store(it, s):
                here = at(it, s)
                wait(sp, out_ready, count(it, s, plus=1))
                sp.dma_start(out[bass.ds(here, 1), :, :].rearrange("b p n -> (b p) n"), out_rows[:, s % O_RING, :]).then_inc(out_stored[s % O_RING], 16)

            for s in range(GROUP):
                load_x(0, s)
            load_w(W_Q)
            load_x(0, GROUP)
            load_x(0, GROUP + 1)
            load_w(W_K)
            with nc.allow_non_contiguous_dma("biases, a column for each chunk of features"):
                sp.dma_start(bias_qk[:, 0:C], bq.rearrange("(c p) -> p c", p=P)).then_inc(b_loaded, 16)
                sp.dma_start(bias_qk[:, C:TILES], bk.rearrange("(c p) -> p c", p=P)).then_inc(b_loaded, 16)
            load_w(W_V)
            sp.dma_start(bv_rows[:], bv.rearrange("(a n) -> a n", a=1).broadcast_to([P, H])).then_inc(b_loaded, 16)
            sp.dma_start(bf_rows[:], bf.rearrange("(a n) -> a n", a=1).broadcast_to([P, H])).then_inc(b_loaded, 16)
            for s in range(GROUP + 2, RING):
                load_x(0, s)
            load_w(W_F)
            for s in range(LEAD_ADJ):
                load_adj(0, s)
            for s in range(RING, LEAD):
                load_x(0, s)
            loops = (B - LEAD) // RING
            with sp.Fori(0, loops) as it:
                for s in range(RING):
                    store(it, s)
                    load_x(it, s + LEAD)
                    load_adj(it, s + LEAD_ADJ)
            for s in range(RING * loops, B):
                store(0, s)
                load_x(0, s + LEAD)
                load_adj(0, s + LEAD_ADJ)
            for i in range(O_RING):
                sp.wait_ge(out_stored[i], 16 * (B // O_RING))

        @block.gpsimd
        def _(pool):
            pool.memset(ident[:], 0.0).then_inc(zeroed, 1)
            pool.memset(minus_half[:], -0.5).then_inc(consts_ready, 1)
            pool.wait_ge(zeroed, 1)
            pool.affine_select(out=ident[:], in_=ident[:], compare_op=ALU.not_equal, fill=1.0, base=0,
                               pattern=[[-1, P]], channel_multiplier=1).then_inc(consts_ready, 1)
            pool.wait_ge(consts_ready, 2)

            def norm_factors(it, s):
                if not inside(it, s):
                    return
                r = s % N_RING
                wait(pool, h_ready, count(it, s, plus=1 - N_RING))
                wait(pool, var_ready, count(it, s, plus=1))
                pool.tensor_tensor(rstd[:, r, :], var_eps[:, r, :], minus_half[:], ALU.pow).then_inc(rstd_done, 1)
                wait(pool, rstd_done, count(it, s, plus=1))
                pool.sem_inc(pool_passed)
                pool.tensor_scalar(shift[:, r, :], mean_var[:, r, 0:1], rstd[:, r, :], -1.0, ALU.mult, ALU.mult).then_inc(norm_ready, 1)

            def make_mask(it, s):
                if not inside(it, s):
                    return
                wait(pool, masked, count(it, s - 2, NH, NH))
                wait(pool, adj_loaded[s // GROUP % 2], lap(it, s) * 16)
                pool.sem_inc(pool_passed)
                pool.tensor_scalar(mask[:, s % 2, :], adj_in[:, s // GROUP % 2, s % GROUP, :], -1.0,
                                   MASKED / ROOT, ALU.add, ALU.mult).then_inc(mask_ready, 1)

            def add_bf(it, s):
                if not inside(it, s):
                    return
                if isinstance(it, int) and s == 0:
                    pool.wait_ge(b_loaded, 64)
                wait(pool, out_ready, count(it, s, plus=1 - RING))
                wait(pool, x_loaded[s % RING], lap(it, s) * 16)
                pool.tensor_tensor(x_bf[:, s % RING, :], x_in[:, s % RING, :], bf_rows[:], ALU.add).then_inc(x_bf_ready, 1)

            def normalise(it, s):
                if not inside(it, s):
                    return
                wait(pool, pT_ready, count(it, s))
                wait(pool, inv_ready, count(it, s, plus=1))
                pool.sem_inc(pool_passed)
                for h in range(NH):
                    last = pool.tensor_scalar(probs_n[:, h, :], probs[:, h, :], inv_sum[:, h:h + 1], 1.0,
                                              ALU.mult, ALU.mult)
                last.then_inc(probs_ready, 1)

            def step(it, s):
                normalise(it, s)
                make_mask(it, s + 2)
                add_bf(it, s + LEAD_X)
                norm_factors(it, s + LEAD_M)

            run(pool, step)

        @block.scalar
        def _(act):
            act.wait_ge(consts_ready, 2)
            act.activation(table_probe[:], minus_half[:], ACT.Exp)
            zero_k(act, 0, 1)

            def layer_norm(it, s):
                if not inside(it, s):
                    return
                wait(act, hT_ready, count(it, s, plus=-1))
                wait(act, x_loaded[s % RING], lap(it, s) * 16)
                wait(act, norm_ready, count(it, s, plus=1))
                act.activation(h_rows[:, s % 2, :], x_in[:, s % RING, :], ACT.Relu,
                               bias=shift[:, s % N_RING, :], scale=rstd[:, s % N_RING, :]).then_inc(h_ready, 1)

            def exps(it, s):
                if not inside(it, s):
                    return
                wait(act, probs_ready, count(it, s))
                for h in range(NH):
                    wait(act, masked, count(it, s, NH, h + 1))
                    last = act.activation(probs[:, h, :], neg_scores[:, h, :], ACT.Exp,
                                          bias=neg_max[:, h:h + 1], scale=-1.0, accum_out=row_sum[:, h:h + 1])
                last.then_inc(exp_done, 1)

            def hT_to_hi(it, s):
                if not inside(it, s):
                    return
                wait(act, hT_ready, count(it, s, plus=1))
                act.activation(hT_hi[:, :, s % RING, :], hT_bank(it, s)[:, 0:H].rearrange("p (c n) -> p c n", c=C),
                               ACT.Copy).then_inc(hT_hi_ready, 1)

            def drain_qk(it, s):
                for place, (t, number) in enumerate(group_tiles(it, s)):
                    if isinstance(it, int) and number == 0:
                        act.wait_ge(b_loaded, 64)
                    wait(act, qk_ready, number + 1)
                    kind, c = TILE[t]
                    for rows, to in tile_parts(it, s, t, HI):
                        act.activation(to, tile_bank(it, s, place)[rows, :].rearrange("p (j n) -> p j n", j=GROUP),
                                       ACT.Identity, bias=bias_qk[rows, kind * C + c:kind * C + c + 1]).then_inc(qk_hi_ready, 1)

            def drain_pT(it, s):
                if not inside(it, s):
                    return
                wait(act, pT_ready, count(it, s, plus=1))
                act.activation(pT[:, s % 2, :, :].rearrange("p (b h) n -> p b (h n)", b=2), ps_pT[:, :, 0:HALF * P],
                               ACT.Copy).then_inc(pT_drained, 1)

            def step(it, s):
                if filled(it, s - 1):
                    exps(it, s)
                layer_norm(it, s + LEAD_N)
                drain_qk(it, s)
                hT_to_hi(it, s + LEAD_H)
                if not filled(it, s):
                    exps(it, s + 1)
                drain_pT(it, s)
                if isinstance(it, int) and s in SPLIT_AT:
                    i = SPLIT_AT.index(s)
                    act.wait_ge(w_loaded[i], 16)
                    act.activation(w_hi[:, i, :, :], w_raw[:, i, :, :], ACT.Copy).then_inc(w_hi_ready, 1)
                if isinstance(it, int) and s == ZERO_AT:
                    zero_k(act, 1, 1)

            run(act, step)

        @block.tensor
        def _(pe):
            pe.wait_ge(consts_ready, 2)

            def three_passes(o, hi, lo, w_hi_part, w_lo_part, stationary_w=False):
                n = 0
                for c in range(C):
                    for a, w in ((hi, w_hi_part), (hi, w_lo_part), (lo, w_hi_part)):
                        lhsT, rhs = (w(c), a(c)) if stationary_w else (a(c), w(c))
                        last = pe.matmul(o, lhsT, rhs, start=(n == 0), stop=(n == 3 * C - 1))
                        n += 1
                return last

            def scores(it, s):
                if not inside(it, s):
                    return
                g = s // GROUP
                if s % GROUP == 0:
                    if isinstance(it, int) and s == 0:
                        pe.wait_ge(k_zeroed, 4)
                    wait(pe, qk_drained, it * (2 * TILES) + (g + 1) * TILES)
                wait(pe, masked, count(it, s, NH))
                j = (s % GROUP) * P
                for c in range(C):
                    o = ps_sc[c // 2][:, c % 2 * 2 * P:(c % 2 + 1) * 2 * P]
                    for n, (a, b) in enumerate(((HI, HI), (HI, LO), (LO, HI))):
                        last = pe.matmul(o, q_parts[:, a, c, g % 2, j:j + P], k_parts[:, g % 2, b, c, s % GROUP, :, :],
                                         start=(n == 0), stop=(n == 2))
                last.then_inc(scores_ready, 1)

            def context(it, s):
                if not inside(it, s):
                    return
                wait(pe, v_drained, count(it, s, plus=1))
                wait(pe, cT_split, count(it, s))
                wait(pe, pT_drained, count(it, s, plus=1))
                for h in range(NH):
                    o = D * (h % 2)
                    last = pe.matmul(ps_ctx[o:o + D, (h // 2) * P:(h // 2 + 1) * P],
                                     v_rows[:, s % V_RING, h * D:(h + 1) * D], pT[:, s % 2, h, :],
                                     start=True, stop=True)
                last.then_inc(ctx_ready, 1)

            def transpose_h(it, s):
                if not inside(it, s):
                    return
                wait(pe, hT_split, count(it, s - (isinstance(it, int) and s < LEAD_H)))
                wait(pe, h_ready, count(it, s, plus=1))
                for c in range(C):
                    last = pe.transpose(hT_bank(it, s)[:, c * P:(c + 1) * P], h_rows[:, s % 2, c * P:(c + 1) * P], ident[:])
                last.then_inc(hT_ready, 1)

            def project_v(it, s):
                if not inside(it, s):
                    return
                step_s = s - LEAD_V
                if isinstance(it, int) and s == 0:
                    pe.wait_ge(w_lo_ready, W_V + 1)
                wait(pe, v_drained, count(it, s))
                if out_bank(step_s - 1) is ps_v:
                    wait(pe, out_ready, count(it, step_s - 1))
                else:
                    wait(pe, out_ready, count(it, step_s - 2))
                if not isinstance(it, int) or step_s > 1:
                    wait(pe, qk_drained, tiles_before(it, step_s, 1))
                wait(pe, hT_split, count(it, s, plus=1))
                r = s % RING
                three_passes(ps_v[:, 0:H], lambda c: hT_hi[:, c, r, :], lambda c: hT_lo[:, c, r, :],
                             lambda c: w_hi[:, W_V, c, :], lambda c: w_lo[:, W_V, c, :]).then_inc(v_ready, 1)

            def project_qk(it, s):
                g = s // GROUP + 1
                slots = slice(g % 2 * GROUP, g % 2 * GROUP + GROUP)
                for place, (t, number) in enumerate(group_tiles(it, s)):
                    if t == 0:
                        wait(pe, hT_split, count(it, g * GROUP, plus=GROUP))
                    if not isinstance(it, int) or s >= 0:
                        if place:
                            wait(pe, v_drained, count(it, s + LEAD_V, plus=1))
                        else:
                            wait(pe, qk_drained, tiles_before(it, s, 0))
                            wait(pe, out_ready, count(it, s - 1))
                    elif s == -1:
                        wait(pe, qk_drained, 1)
                    i, m = (W_Q, W_K)[TILE[t][0]], TILE[t][1]
                    if isinstance(it, int) and g == 0:
                        pe.wait_ge(w_lo_ready, i + 1)
                    cols = slice(m * P, (m + 1) * P)
                    three_passes(tile_bank(it, s, place)[:, :],
                                 lambda c: hT_hi[:, c, slots, :], lambda c: hT_lo[:, c, slots, :],
                                 lambda c: w_hi[:, i, c, cols], lambda c: w_lo[:, i, c, cols],
                                 stationary_w=True).then_inc(qk_ready, 1)

            def project_out(it, s):
                if not inside(it, s):
                    return
                if isinstance(it, int) and s == 0:
                    pe.wait_ge(w_lo_ready, W_F + 1)
                tiles = group_tiles(it, s + 1)
                if out_bank(s + 1) is ps_v and inside(it, s + 1 + LEAD_V):
                    wait(pe, v_drained, count(it, s + 1 + LEAD_V, plus=1))
                elif tiles:
                    wait(pe, qk_drained, tiles[0][1] + 1)
                wait(pe, out_ready, count(it, s))
                wait(pe, cT_split, count(it, s, plus=1))
                r = s % 2
                three_passes(out_bank(s + 1)[:, 0:H], lambda c: cT_hi[:, r, c, :], lambda c: cT_lo[:, r, c, :],
                             lambda c: w_hi[:, W_F, c, :], lambda c: w_lo[:, W_F, c, :]).then_inc(proj_ready, 1)

            def transpose_probs(it, s):
                if not inside(it, s):
                    return
                wait(pe, pT_drained, count(it, s))
                wait(pe, probs_ready, count(it, s, plus=1))
                for h in range(NH):
                    c = (h % HALF) * P
                    last = pe.transpose(ps_pT[:, h // HALF, c:c + P], probs_n[:, h, :], ident[:])
                last.then_inc(pT_ready, 1)

            def step(it, s):
                if isinstance(it, int) and s < 1:
                    project_qk(it, s)
                    project_v(it, s + LEAD_V)
                    transpose_h(it, s + LEAD_H)
                    scores(it, s + 1)
                    transpose_probs(it, s)
                elif filled(it, s):
                    project_v(it, s + LEAD_V)
                    context(it, s - 1)
                    project_qk(it, s)
                    transpose_h(it, s + LEAD_H)
                    project_out(it, s - 1)
                    transpose_probs(it, s)
                    scores(it, s + 1)
                else:
                    scores(it, s + 1)
                    context(it, s - 1)
                    project_v(it, s + LEAD_V)
                    transpose_h(it, s + LEAD_H)
                    project_out(it, s - 1)
                    transpose_probs(it, s)

            run(pe, step)

        @block.vector
        def _(dve):
            dve.wait_ge(consts_ready, 2)
            zero_k(dve, 0, 0)

            def row_moments(it, s):
                if not inside(it, s):
                    return
                r = s % N_RING
                wait(dve, norm_ready, count(it, s, plus=1 - N_RING))
                wait(dve, x_loaded[s % RING], lap(it, s) * 16)
                dve.bn_stats(bn[:, r, :], x_in[:, s % RING, :]).then_inc(bn_done, 1)
                wait(dve, bn_done, count(it, s, plus=1))
                dve.sem_inc(dve_passed)
                dve.bn_aggr(mean_var[:, r, :], bn[:, r, :]).then_inc(moments, 1)
                wait(dve, moments, count(it, s, plus=1))
                dve.tensor_scalar(var_eps[:, r, :], mean_var[:, r, 1:2], NORM_EPS, None, ALU.add).then_inc(var_ready, 1)

            def mask_and_max(it, s):
                if not inside(it, s):
                    return
                wait(dve, mask_ready, count(it, s, plus=1))
                wait(dve, scores_ready, count(it, s, plus=1))
                dve.sem_inc(dve_passed)
                for h in range(NH):
                    dve.tensor_tensor_reduce(neg_scores[:, h, :], head_scores(h),
                                             mask[:, s % 2, :], -ROOT, 3.0e38, ALU.add, ALU.min,
                                             neg_max[:, h:h + 1]).then_inc(masked, 1)

            def split_context(it, s):
                if not inside(it, s):
                    return
                r = s % 2
                wait(dve, ctx_ready, count(it, s, plus=1))
                dve.tensor_copy(cT_hi[:, r, :, :].rearrange("p c n -> p (c n)"), ps_ctx[:, 0:H]).then_inc(cT_hi_ready, 1)
                wait(dve, cT_hi_ready, count(it, s, plus=1))
                dve.tensor_tensor(cT_lo[:, r, :, :].rearrange("p c n -> p (c n)"), ps_ctx[:, 0:H],
                                  cT_hi[:, r, :, :].bitcast(F32).rearrange("p c n -> p (c n)"),
                                  ALU.subtract).then_inc(cT_split, 1)

            def invert_sums(it, s):
                if not inside(it, s):
                    return
                wait(dve, exp_done, count(it, s, plus=1))
                dve.reciprocal(inv_sum[:], row_sum[:]).then_inc(inv_ready, 1)

            def hT_to_lo(it, s):
                if not inside(it, s):
                    return
                wait(dve, hT_hi_ready, count(it, s, plus=1))
                dve.tensor_tensor(hT_lo[:, :, s % RING, :], hT_bank(it, s)[:, 0:H].rearrange("p (c n) -> p c n", c=C),
                                  hT_hi[:, :, s % RING, :].bitcast(F32), ALU.subtract).then_inc(hT_split, 1)

            def qk_to_lo(it, s):
                for place, (t, number) in enumerate(group_tiles(it, s)):
                    kind, c = TILE[t]
                    for n, ((rows, to), (_, hi)) in enumerate(zip(tile_parts(it, s, t, LO), tile_parts(it, s, t, HI))):
                        wait(dve, qk_hi_ready, hi_count(it, s, t, n + 1))
                        last = dve.scalar_tensor_tensor(to, tile_bank(it, s, place)[rows, :].rearrange("p (j n) -> p j n", j=GROUP),
                                                        bias_qk[rows, kind * C + c:kind * C + c + 1], hi.bitcast(F32),
                                                        ALU.add, ALU.subtract)
                    last.then_inc(qk_drained, 1)

            def drain_v(it, s):
                if not inside(it, s):
                    return
                if isinstance(it, int) and s == 0:
                    dve.wait_ge(b_loaded, 64)
                wait(dve, v_ready, count(it, s, plus=1))
                dve.tensor_tensor(v_rows[:, s % V_RING, :], ps_v[:, 0:H], bv_rows[:], ALU.add).then_inc(v_drained, 1)

            def residual(it, s):
                if not inside(it, s):
                    return
                wait(dve, x_bf_ready, count(it, s, plus=1))
                wait(dve, out_stored[s % O_RING], (lap(it, s, O_RING) - 1) * 16)
                wait(dve, proj_ready, count(it, s, plus=1))
                dve.tensor_tensor(out_rows[:, s % O_RING, :], out_bank(s + 1)[:, 0:H], x_bf[:, s % RING, :],
                                  ALU.add).then_inc(out_ready, 1)

            def step(it, s):
                if isinstance(it, int) and s < 1:
                    if s + LEAD_M < GROUP:
                        row_moments(it, s + LEAD_M)
                    qk_to_lo(it, s)
                    drain_v(it, s + LEAD_V)
                    invert_sums(it, s)
                    hT_to_lo(it, s + LEAD_H)
                    mask_and_max(it, s + 1)
                elif filled(it, s):
                    drain_v(it, s + LEAD_V)
                    invert_sums(it, s)
                    split_context(it, s - 1)
                    qk_to_lo(it, s)
                    residual(it, s - 1)
                    hT_to_lo(it, s + LEAD_H)
                    mask_and_max(it, s + 1)
                else:
                    invert_sums(it, s)
                    mask_and_max(it, s + 1)
                    split_context(it, s - 1)
                    drain_v(it, s + LEAD_V)
                    hT_to_lo(it, s + LEAD_H)
                    residual(it, s - 1)
                if not isinstance(it, int) or s + LEAD_M >= GROUP:
                    row_moments(it, s + LEAD_M)
                if isinstance(it, int) and s in SPLIT_AT:
                    i = SPLIT_AT.index(s)
                    dve.wait_ge(w_hi_ready, i + 1)
                    dve.tensor_tensor(w_lo[:, i, :, :], w_raw[:, i, :, :], w_hi[:, i, :, :].bitcast(F32),
                                      ALU.subtract).then_inc(w_lo_ready, 1)

                if isinstance(it, int) and s == ZERO_AT:
                    zero_k(dve, 1, 0)

            run(dve, step)


_INS = ["x", "adj", "L0_gnn_Wq", "L0_gnn_bq", "L0_gnn_Wk", "L0_gnn_bk", "L0_gnn_Wv", "L0_gnn_bv", "L0_gnn_Wf", "L0_gnn_bf"]


def kernel(**inputs):
    import numpy as _np
    import concourse.bacc as _bacc
    from concourse import mybir as _mybir
    from concourse.bass_utils import run_bass_kernel_spmd as _run

    nc = _bacc.Bacc("TRN2", target_bir_lowering=False, num_devices=1)
    arrays, args = {}, []
    for name in _INS:
        a = _np.asarray(inputs[name])
        if name == "adj":
            a = a.transpose(1, 0, 2)
        a = _np.ascontiguousarray(a)
        arrays[f"in_{name}_dram"] = a
        args.append(nc.dram_tensor(f"in_{name}_dram", a.shape, _mybir.dt.from_np(a.dtype), kind="ExternalInput").ap())
    shape = inputs["x"].shape
    args.append(nc.dram_tensor("out_0_dram", shape, _mybir.dt.from_np(_np.dtype("float32")), kind="ExternalOutput").ap())
    bass_preln_graph_attention(nc, *args)
    r = _run(nc, [arrays], core_ids=[0])
    return r.results[0]["out_0_dram"]
```
